# Optimizing a Trainium2 kernel written in Bass

```python
import numpy as np
import jax
import jax.numpy as jnp

def _softmax(x, axis=-1):
    return jax.nn.softmax(x, axis=axis)

def _gelu(x):
    return jax.nn.gelu(x, approximate=True)

def _silu(x):
    return jax.nn.silu(x)

def _sigmoid(x):
    return jax.nn.sigmoid(x)

def _layernorm(x, axis=-1, eps=1e-05):
    m = jnp.mean(x, axis=axis, keepdims=True)
    v = jnp.var(x, axis=axis, keepdims=True)
    return (x - m) / jnp.sqrt(v + eps)

def _scatter_add(tgt, idx, src, axis=0):
    return tgt.at[idx].add(src)

def _segment_sum(src, seg, n):
    return jax.ops.segment_sum(src, seg, n)
kernel_name = 'mk_xattn_seq_d2_seqx_r2_c2e7a7'

def setup_inputs(seed: int=0):
    np.random.seed(seed)
    _w = jnp.asarray

    def _rec_inputs():
        import jax
        import jax.numpy as jnp
        _rk = jax.random.key(seed)
        x = -0.000125 + 0.9999 * jax.random.normal(jax.random.fold_in(_rk, 1), (16, 256, 2048), jnp.float32)
        _lenS = 256 - jax.random.randint(jax.random.fold_in(_rk, 7), (16,), 0, max(1, 256 // 4) + 1, jnp.int32)
        _lenS2 = 256 - jax.random.randint(jax.random.fold_in(_rk, 8), (16,), 0, max(1, 256 // 4) + 1, jnp.int32)
        _ctx_4096P = jax.random.normal(jax.random.fold_in(_rk, 11), (16, 16, 2048), jnp.float32)
        _ctx_4096c = jax.random.dirichlet(jax.random.fold_in(_rk, 511), 0.3 * jnp.ones((16,), jnp.float32), (16, 256))
        _ctx_4096t = jnp.einsum('bsk,bkd->bsd', _ctx_4096c, _ctx_4096P)
        _ctx_4096t = _ctx_4096t * jax.lax.rsqrt(jnp.mean(jnp.square(_ctx_4096t)) + 1e-12) * 0.953939
        ctx_4096 = -1.52775e-05 + 0.999936 * (_ctx_4096t + 0.3 * jax.random.normal(jax.random.fold_in(_rk, 611), (16, 256, 2048), jnp.float32))
        _validS = jnp.arange(256)[None, :] < _lenS[:, None]
        _validS2 = jnp.arange(256)[None, :] < _lenS2[:, None]
        _causal = jnp.tril(jnp.ones((256, 256), dtype=bool))
        mask_Bx1x4096_ff1 = jnp.where(jnp.ones((16, 1, 2048), dtype=bool), 1.0, 0.0).astype(jnp.float32)
        return (x, ctx_4096, mask_Bx1x4096_ff1)
    x, ctx_4096, mask_Bx1x4096_ff1 = _rec_inputs()

    def _L0_xattn_setup():
        import jax, jax.numpy as jnp
        import numpy as np
        NUM_HEADS = 8
        EPS = 1e-05

        def _conv1x1(W, b, t):
            return jnp.einsum('oc,bcl->bol', W, t) + b[None, :, None]
        key = jax.random.key(seed)
        ks = jax.random.split(key, 12)
        B, C, E, L = (16, 256, 256, 2048)
        s = lambda k, shape, sc=1.0: jax.random.normal(k, shape, dtype=jnp.float32) * sc
        return {'x': s(ks[0], (B, E, L)), 'y': s(ks[1], (B, C, L)), 'Wq': s(ks[2], (E, C), 0.02), 'bq': jnp.zeros((E,), jnp.float32), 'Wk': s(ks[3], (E, C), 0.02), 'bk': jnp.zeros((E,), jnp.float32), 'Wv': s(ks[4], (E, E), 0.02), 'bv': jnp.zeros((E,), jnp.float32), 'Wo': s(ks[5], (E, E), 0.02), 'bo': jnp.zeros((E,), jnp.float32), 'gn_w': jnp.ones((E,), jnp.float32), 'gn_b': jnp.zeros((E,), jnp.float32)}
    _L0_xattn_all = _L0_xattn_setup()
    _L0_xattn_in = {k: v for k, v in _L0_xattn_all.items() if k in ('Wq', 'bq', 'Wk', 'bk', 'Wv', 'bv', 'Wo', 'bo', 'gn_w', 'gn_b')}
    del _L0_xattn_all

    def _L1_xattn_setup():
        import jax, jax.numpy as jnp
        import numpy as np
        NUM_HEADS = 8
        CHUNK = 64
        EPS = 1e-05
        NEG = -1000000000.0

        def _chunk_attn(q, k, v, masks, W_in, b_in, W_out, b_out):
            N, C, T = q.shape
            H, Dh = (NUM_HEADS, C // NUM_HEADS)
            nc = T // CHUNK
            Wq, Wk, Wv = jnp.split(W_in, 3, axis=0)
            bq, bk, bv = jnp.split(b_in, 3, axis=0)

            def proj(t, W, b):
                t = t.transpose(0, 2, 1) @ W.T + b
                return t.reshape(N, nc, CHUNK, H, Dh)
            qh = proj(q, Wq, bq)
            kh = proj(k, Wk, bk)
            vh = proj(v, Wv, bv)
            scale = 1.0 / jnp.sqrt(jnp.asarray(Dh, q.dtype))
            scores = jnp.einsum('bnqhd,bnkhd->bnhqk', qh, kh) * scale
            km = masks[:, 0, :].reshape(N, nc, CHUNK)
            scores = scores + jnp.where(km[:, :, None, None, :] > 0, 0.0, NEG)
            attn = jax.nn.softmax(scores, axis=-1)
            out = jnp.einsum('bnhqk,bnkhd->bnqhd', attn, vh).reshape(N, T, C)
            out = out @ W_out.T + b_out
            out = out.transpose(0, 2, 1) * masks
            return out
        key = jax.random.key(seed)
        ks = jax.random.split(key, 8)
        N, C, T = (4, 256, 2048)
        x = jax.random.normal(ks[0], (N, C, T), dtype=jnp.float32)
        q = jax.random.normal(ks[1], (N, C, T), dtype=jnp.float32)
        k = jax.random.normal(ks[2], (N, C, T), dtype=jnp.float32)
        v = jax.random.normal(ks[3], (N, C, T), dtype=jnp.float32)
        masks = jnp.ones((N, 1, T), dtype=jnp.float32)
        s = 1.0 / np.sqrt(C)
        W_in = jax.random.normal(ks[4], (3 * C, C), dtype=jnp.float32) * s
        b_in = jnp.zeros((3 * C,), dtype=jnp.float32)
        W_out = jax.random.normal(ks[5], (C, C), dtype=jnp.float32) * s
        b_out = jnp.zeros((C,), dtype=jnp.float32)
        return {'x': x, 'q': q, 'k': k, 'v': v, 'masks': masks, 'W_in': W_in, 'b_in': b_in, 'W_out': W_out, 'b_out': b_out}
    _L1_xattn_all = _L1_xattn_setup()
    _L1_xattn_in = {k: v for k, v in _L1_xattn_all.items() if k in ('W_in', 'b_in', 'W_out', 'b_out')}
    del _L1_xattn_all
    return {'x': x, 'ctx_4096': ctx_4096, 'mask_Bx1x4096_ff1': mask_Bx1x4096_ff1, 'L0_xattn_Wq': _L0_xattn_in['Wq'], 'L0_xattn_bq': _L0_xattn_in['bq'], 'L0_xattn_Wk': _L0_xattn_in['Wk'], 'L0_xattn_bk': _L0_xattn_in['bk'], 'L0_xattn_Wv': _L0_xattn_in['Wv'], 'L0_xattn_bv': _L0_xattn_in['bv'], 'L0_xattn_Wo': _L0_xattn_in['Wo'], 'L0_xattn_bo': _L0_xattn_in['bo'], 'L0_xattn_gn_w': _L0_xattn_in['gn_w'], 'L0_xattn_gn_b': _L0_xattn_in['gn_b'], 'L1_xattn_W_in': _L1_xattn_in['W_in'], 'L1_xattn_b_in': _L1_xattn_in['b_in'], 'L1_xattn_W_out': _L1_xattn_in['W_out'], 'L1_xattn_b_out': _L1_xattn_in['b_out']}

def reference(x, ctx_4096, mask_Bx1x4096_ff1, L0_xattn_Wq, L0_xattn_bq, L0_xattn_Wk, L0_xattn_bk, L0_xattn_Wv, L0_xattn_bv, L0_xattn_Wo, L0_xattn_bo, L0_xattn_gn_w, L0_xattn_gn_b, L1_xattn_W_in, L1_xattn_b_in, L1_xattn_W_out, L1_xattn_b_out):
    import jax
    import jax.numpy as jnp

    def _L0_xattn_ref(x, y, Wq, bq, Wk, bk, Wv, bv, Wo, bo, gn_w, gn_b):
        import jax, jax.numpy as jnp
        import numpy as np
        NUM_HEADS = 8
        EPS = 1e-05

        def _conv1x1(W, b, t):
            return jnp.einsum('oc,bcl->bol', W, t) + b[None, :, None]
        B, E, Lx = x.shape
        H = NUM_HEADS
        Dh = E // H
        q = _conv1x1(Wq, bq, y).reshape(B, H, Dh, -1)
        k = _conv1x1(Wk, bk, y).reshape(B, H, Dh, -1)
        v = _conv1x1(Wv, bv, x).reshape(B, H, Dh, Lx)
        scores = jnp.einsum('bhdl,bhel->bhde', q, k) / jnp.sqrt(jnp.float32(E))
        attn = jax.nn.softmax(scores, axis=-1)
        out = jnp.einsum('bhde,bhel->bhdl', attn, v).reshape(B, E, Lx)
        o = _conv1x1(Wo, bo, out) + x
        mu = jnp.mean(o, axis=(1, 2), keepdims=True)
        var = jnp.var(o, axis=(1, 2), keepdims=True)
        o_hat = (o - mu) * jax.lax.rsqrt(var + EPS)
        return o_hat * gn_w[None, :, None] + gn_b[None, :, None]

    def _L1_xattn_ref(x, q, k, v, masks, W_in, b_in, W_out, b_out):
        import jax, jax.numpy as jnp
        import numpy as np
        NUM_HEADS = 8
        CHUNK = 64
        EPS = 1e-05
        NEG = -1000000000.0

        def _chunk_attn(q, k, v, masks, W_in, b_in, W_out, b_out):
            N, C, T = q.shape
            H, Dh = (NUM_HEADS, C // NUM_HEADS)
            nc = T // CHUNK
            Wq, Wk, Wv = jnp.split(W_in, 3, axis=0)
            bq, bk, bv = jnp.split(b_in, 3, axis=0)

            def proj(t, W, b):
                t = t.transpose(0, 2, 1) @ W.T + b
                return t.reshape(N, nc, CHUNK, H, Dh)
            qh = proj(q, Wq, bq)
            kh = proj(k, Wk, bk)
            vh = proj(v, Wv, bv)
            scale = 1.0 / jnp.sqrt(jnp.asarray(Dh, q.dtype))
            scores = jnp.einsum('bnqhd,bnkhd->bnhqk', qh, kh) * scale
            km = masks[:, 0, :].reshape(N, nc, CHUNK)
            scores = scores + jnp.where(km[:, :, None, None, :] > 0, 0.0, NEG)
            attn = jax.nn.softmax(scores, axis=-1)
            out = jnp.einsum('bnhqk,bnkhd->bnqhd', attn, vh).reshape(N, T, C)
            out = out @ W_out.T + b_out
            out = out.transpose(0, 2, 1) * masks
            return out
        out = _chunk_attn(q, k, v, masks, W_in, b_in, W_out, b_out) + x
        mu = jnp.mean(out, axis=2, keepdims=True)
        var = jnp.mean(jnp.square(out - mu), axis=2, keepdims=True)
        return (out - mu) * jax.lax.rsqrt(var + EPS)
    x = _L0_xattn_ref(x, ctx_4096, L0_xattn_Wq, L0_xattn_bq, L0_xattn_Wk, L0_xattn_bk, L0_xattn_Wv, L0_xattn_bv, L0_xattn_Wo, L0_xattn_bo, L0_xattn_gn_w, L0_xattn_gn_b)
    x = _L1_xattn_ref(x, ctx_4096, ctx_4096, ctx_4096, mask_Bx1x4096_ff1, L1_xattn_W_in, L1_xattn_b_in, L1_xattn_W_out, L1_xattn_b_out)
    return x

_drawn_inputs = setup_inputs


def setup_inputs(seed=0):
    import zlib

    import numpy as np

    out = dict(_drawn_inputs(seed))
    spreads = {'L0_xattn_bq': (0.0, 0.1),
     'L0_xattn_bk': (0.0, 0.1),
     'L0_xattn_bv': (0.0, 0.8),
     'L0_xattn_bo': (0.0, 0.8),
     'L0_xattn_gn_w': (1.0, 0.2),
     'L0_xattn_gn_b': (0.0, 0.8),
     'L1_xattn_b_in': (0.0, 0.443),
     'L1_xattn_b_out': (0.0, 0.8)}
    factors = {}
    for name, (base, spread) in spreads.items():
        noise = np.random.default_rng([zlib.crc32(name.encode()), seed]).standard_normal(out[name].shape)
        drawn = base * np.exp(spread * noise) if base else spread * noise
        out[name] = jnp.asarray(drawn.astype(out[name].dtype))
    for name, factor in factors.items():
        out[name] = (out[name] * factor).astype(out[name].dtype)
    return out
```

```python
import concourse.bass as bass
from concourse import mybir
from contextlib import ExitStack

F32 = mybir.dt.float32
F32R = mybir.dt.float32r
BF16 = mybir.dt.bfloat16
ALU = mybir.AluOpType
ACT = mybir.ActivationFunctionType
AX = mybir.AxisListType

P = 128
SAMPLES, E, L = 16, 256, 2048
HEADS, CHUNK, DH = 8, 64, 32
HALVES = E // P
BT = 512
BLOCKS = L // BT
PAIRS = BT // P
SLOTS = BLOCKS * PAIRS
HP = HEADS // 2
RING = 4
LAG = 2
EPS = 1e-5
NEG = -1e9
SCALE0 = 1.0 / E ** 0.5
SCALE1 = 1.0 / DH ** 0.5
OFF_HEAD = -3e38
Q_W, K_W, V_W, O_W = range(4)
C_IDENT, C_HEAD, C_RESID, C_MEAN, C_NEG = 0, P, 2 * P, 2 * P + 2 * E, 3 * P + 2 * E
C_ALL = C_NEG + P
V_BQ0, V_BV0, V_BO0, V_GW, V_GB, V_BQ1, V_BK1, V_BV1, V_BO1 = range(9)

S_SPLIT_T, S_GRAM, S_HL, S_HLT, S_SUM, S_T1, S_SC, S_U, S_M, S_X, S_MX = 0, 1, 4, 5, 6, 7, 8, 10, 11, 11, 12
T_X1, T_Z, T_Z_STATS, T_STAT, T_FINAL, T_STORE = 1, 3, 4, 8, 9, 9


def build(nc, x, ctx, ctx_t, mask, w0, w1, cols, bk0, consts, out):
    x_d = x.rearrange("n (h p) t -> n p h t", p=P)
    y_d = ctx.rearrange("n (h p) t -> n p h t", p=P)
    yt_d = ctx_t.rearrange("n (l p) c -> n p l c", p=P)
    mask_rows_d = mask.rearrange("n a (r c k) -> n (a c) r k", c=2, k=CHUNK)
    out_d = out.rearrange("n (h p) t -> n p h t", p=P)

    es = ExitStack()
    with es:
        def sb(name, shape, dt=F32):
            return es.enter_context(nc.sbuf_tensor(name, shape, dt))

        def sem(name):
            return es.enter_context(nc.semaphore(name))

        cst = sb("cst", [P, C_ALL])
        ident, head_mask = cst[:, C_IDENT:C_IDENT + P], cst[:, C_HEAD:C_HEAD + P]
        resid = cst[:, C_RESID:C_RESID + 2 * E].rearrange("p (j o) -> p j o", j=HALVES)
        mean_mat = cst[:, C_MEAN:C_MEAN + P]
        neg_sel = sb("neg_sel", [P, P], BF16)
        w0_sb = sb("w0_sb", [P, 4, HALVES, E])
        w1_hi = sb("w1_hi", [P, 4, HALVES, E], F32R)
        w1_lo = sb("w1_lo", [P, 4, HALVES, E], F32R)
        col = sb("col", [P, 9, HALVES])
        bk_row = sb("bk_row", [P, E])
        bk_l = sb("bk_l", [P, E])
        c1 = sb("c1", [P, HALVES])
        y_raw = sb("y_raw", [P, 2, HALVES, BT])
        yt_raw = sb("yt_raw", [P, 2, PAIRS, E])
        x_raw = sb("x_raw", [P, 2, HALVES, BT])
        mask_b = sb("mask_b", [P, 2, BT])
        mask_r = sb("mask_r", [6, 2, PAIRS, CHUNK])
        y_hi = sb("y_hi", [P, 2, HALVES, BT], F32R)
        y_lo = sb("y_lo", [P, 2, HALVES, BT], F32R)
        yt_hl = sb("yt_hl", [P, PAIRS, 2, E], F32R)
        x_hi = sb("x_hi", [P, HALVES, BT], F32R)
        x_lo = sb("x_lo", [P, HALVES, BT], F32R)
        att_hi = sb("att_hi", [P, 2, HALVES, BT], F32R)
        att_lo = sb("att_lo", [P, 2, HALVES, BT], F32R)
        k_s = sb("k_s", [P, HALVES, 2, PAIRS * CHUNK])
        q_st = sb("q_st", [P, 2, HP, PAIRS, 2, CHUNK])
        k_bd = sb("k_bd", [P, 2, HP, 2, PAIRS * CHUNK])
        v_bd = sb("v_bd", [P, 2, PAIRS, 2, HP, 2, DH])
        blocked = sb("blocked", [P, 2, PAIRS, CHUNK], BF16)
        prob = sb("prob", [P, RING, HEADS, CHUNK])
        prob_t = sb("prob_t", [P, 2, HP, P])
        row_max = sb("row_max", [P, RING, HEADS])
        row_sum = sb("row_sum", [P, RING, HEADS])
        row_inv = sb("row_inv", [P, RING, HEADS])
        y_sums = sb("y_sums", [P, HALVES, BLOCKS])
        y_sum = sb("y_sum", [P, HALVES])
        y_sum_b = sb("y_sum_b", [P, HALVES, P])
        work_a = sb("work_a", [P, HALVES, E])
        work_b = sb("work_b", [P, HALVES, E])
        hl = t1 = m_t = work_a
        gram = u0 = work_b
        v_row = sb("v_row", [P, E])
        a0 = sb("a0", [P, HALVES, P])
        a0_max = sb("a0_max", [P, HALVES])
        a0_sum = sb("a0_sum", [P, HALVES])
        m_hi = sb("m_hi", [P, HALVES, E], F32R)
        m_lo = sb("m_lo", [P, HALVES, E], F32R)
        o_bias = sb("o_bias", [P, HALVES])
        o_sb = sb("o_sb", [P, HALVES, L])
        u_sb = sb("u_sb", [P, HALVES, L])
        o_stats = sb("o_stats", [P, HALVES * BLOCKS, 6])
        o_mv = sb("o_mv", [P, 2])
        o_mu = sb("o_mu", [P, 1])
        o_dev = sb("o_dev", [P, 2])
        o_var = sb("o_var", [P, 1])
        o_rstd = sb("o_rstd", [P, 1])
        carrier = sb("carrier", [P, 4])
        power = sb("power", [P, HALVES])
        gn = sb("gn", [P, 2, HALVES])
        z_stats = sb("z_stats", [P, HALVES, BLOCKS, 6])
        z_mv = sb("z_mv", [P, HALVES, 2])
        z_var = sb("z_var", [P, HALVES])
        z_rstd = sb("z_rstd", [P, HALVES])
        z_shift = sb("z_shift", [P, HALVES])

        s_ps = [es.enter_context(nc.psum_tensor(f"s_ps{i}", [P, 512], F32)) for i in range(2)]
        pt_ps = es.enter_context(nc.psum_tensor("pt_ps", [P, HP, P], F32))
        av_ps = es.enter_context(nc.psum_tensor("av_ps", [P, HALVES, P], F32))
        pj_ps = [es.enter_context(nc.psum_tensor(f"pj_ps{i}", [P, 512], F32)) for i in range(2)]
        l0_ps = [es.enter_context(nc.psum_tensor(f"l0_ps{i}", [P, 512], F32)) for i in range(2)]

        weights_in = sem("weights_in")
        zeroed = sem("zeroed")
        consts_done = sem("consts_done")
        w_hi_done = sem("w_hi_done")
        w_lo_done = sem("w_lo_done")
        c1_ready = sem("c1_ready")
        y_in = [sem(f"y_in{i}") for i in range(2)]
        yt_in = [sem(f"yt_in{i}") for i in range(2)]
        x_in = [sem(f"x_in{i}") for i in range(2)]
        mask_b_in = [sem(f"mask_b_in{i}") for i in range(2)]
        mask_r_in = [sem(f"mask_r_in{i}") for i in range(2)]
        k_moved = [sem(f"k_moved{i}") for i in range(2)]
        y_hi_done, y_lo_done = sem("y_hi_done"), sem("y_lo_done")
        yt_hi_done, yt_lo_done = sem("yt_hi_done"), sem("yt_lo_done")
        x_hi_done, x_lo_done = sem("x_hi_done"), sem("x_lo_done")
        blocked_done = sem("blocked_done")
        scores_ready, max_done, shifted = sem("scores_ready"), sem("max_done"), sem("shifted")
        exp_done, sum_done, inv_done = sem("exp_done"), sem("sum_done"), sem("inv_done")
        probs_done, transposed, pt_copied = sem("probs_done"), sem("transposed"), sem("pt_copied")
        av_ready, att_hi_done, att_lo_done = sem("av_ready"), sem("att_hi_done"), sem("att_lo_done")
        qkv_ready, qkv_copied = sem("qkv_ready"), sem("qkv_copied")
        wout_ready, u_done = sem("wout_ready"), sem("u_done")
        gram_ready, hl_copied, gram_half = sem("gram_ready"), sem("hl_copied"), sem("gram_half")
        hlt_ready, gram_done = sem("hlt_ready"), sem("gram_done")
        y_sum_step, y_sum_done = sem("y_sum_step"), sem("y_sum_done")
        t1_ready, t1_done = sem("t1_ready"), sem("t1_done")
        sc0_ready, a0_step, a0_shift, a0_exp, a0_done = sem("sc0_ready"), sem("a0_step"), sem("a0_shift"), sem("a0_exp"), sem("a0_done")
        u0_ready, u0_copied = sem("u0_ready"), sem("u0_copied")
        m_ready, m_done, m_hi_done, m_lo_done, o_bias_done = sem("m_ready"), sem("m_done"), sem("m_hi_done"), sem("m_lo_done"), sem("o_bias_done")
        mx_ready, o_copied, o_stats_done = sem("mx_ready"), sem("o_copied"), sem("o_stats_done")
        o_aggr, mean_ready, dev_step, dev_done, var_ready = sem("o_aggr"), sem("mean_ready"), sem("dev_step"), sem("dev_done"), sem("var_ready")
        gn_step, gn_step2, gn_done, x1_done = sem("gn_step"), sem("gn_step2"), sem("gn_done"), sem("x1_done")
        power_set = sem("power_set")
        blocked_zero, c1_done = sem("blocked_zero"), sem("c1_done")
        z_done, z_stats_done, z_step, z_norm_step, z_rstd_done, z_norm_done = (
            sem("z_done"), sem("z_stats_done"), sem("z_step"), sem("z_norm_step"), sem("z_rstd_done"), sem("z_norm_done"))
        final_done, stored = sem("final_done"), sem("stored")

        def count(n, per, i, inc=1):
            return n * (per * inc) + (i + 1) * inc

        def exists(n, per, i):
            return not isinstance(n, int) or n * per + i >= 0

        def over_samples(eng, body):
            body(0, True, False)
            with eng.Fori(1, SAMPLES - 1) as n:
                body(n, False, False)
            body(SAMPLES - 1, False, True)

        block = es.enter_context(nc.Block())

        @block.sync
        def _(sp):
            def load_y(n, b):
                if exists(n, 4, b - 2):
                    sp.wait_ge(y_hi_done, count(n, 4, b - 2))
                if exists(n, 4, b - 2):
                    sp.wait_ge(y_lo_done, count(n, 4, b - 2))
                sp.dma_start(y_raw[:, b % 2], y_d[n + b // 4][:, :, (b % 4) * BT:(b % 4 + 1) * BT]).then_inc(y_in[b % 2], 16)

            def load_yt(n, q):
                if exists(n, 4, q - 2):
                    sp.wait_ge(yt_hi_done, count(n, 4, q - 2))
                if exists(n, 4, q - 2):
                    sp.wait_ge(yt_lo_done, count(n, 4, q - 2))
                sp.dma_start(yt_raw[:, q % 2], yt_d[n + q // 4][:, (q % 4) * PAIRS:(q % 4 + 1) * PAIRS, :]).then_inc(yt_in[q % 2], 16)

            def load_x(n, q):
                if exists(n, 4, q - 2):
                    sp.wait_ge(x_hi_done, count(n, 4, q - 2))
                if exists(n, 4, q - 2):
                    sp.wait_ge(x_lo_done, count(n, 4, q - 2))
                sp.dma_start(x_raw[:, q % 2], x_d[n + q // 4][:, :, (q % 4) * BT:(q % 4 + 1) * BT]).then_inc(x_in[q % 2], 16)

            def load_mask_b(n, b):
                if exists(n, 8, 2 * (b - 2) + 1):
                    sp.wait_ge(u_done, count(n, 8, 2 * (b - 2) + 1))
                sp.dma_start(mask_b[:, b % 2], mask[n][:, b * BT:(b + 1) * BT].to_broadcast([P, BT])).then_inc(mask_b_in[b % 2], 16)

            def load_mask_r(n, b):
                if exists(n, 4, b - 2):
                    sp.wait_ge(blocked_done, count(n, 4, b - 2))
                for part in range(3):
                    sp.dma_start(mask_r[2 * part:2 * part + 2, b % 2],
                                 mask_rows_d[n + b // 4][:, (b % 4) * PAIRS:(b % 4 + 1) * PAIRS, :]).then_inc(mask_r_in[b % 2], 16)

            def move_k(n, b):
                sp.wait_ge(qkv_copied, count(n, 24, 6 * b + 3))
                for par in range(2):
                    for h in range(2):
                        for c in range(2):
                            sp.dma_start(k_bd[64 * c + 32 * h:64 * c + 32 * h + 32, b % 2, par::2, h, :],
                                         k_s[64 * par + 32 * h:64 * par + 32 * h + 32, :, c, :]).then_inc(k_moved[b % 2], 16)

            def store(n, q):
                sp.wait_ge(final_done, count(n, 4, q))
                sp.dma_start(out_d[n][:, :, q * BT:(q + 1) * BT], o_sb[:, :, q * BT:(q + 1) * BT]).then_inc(stored, 16)

            load_y(0, 0)
            load_mask_r(0, 0)
            sp.dma_start(cst[:, :], consts).then_inc(weights_in, 16)
            sp.dma_start(col[:, :, :], cols).then_inc(weights_in, 16)
            sp.dma_start(u_sb[:, :, :], w1).then_inc(weights_in, 16)
            load_y(0, 1)
            load_yt(0, 0)
            load_yt(0, 1)
            sp.dma_start(w0_sb[:, :, :, :], w0).then_inc(weights_in, 16)
            sp.dma_start(bk_row[:, :], bk0.to_broadcast([P, E])).then_inc(weights_in, 16)
            load_mask_r(0, 1)
            load_y(0, 2)
            load_x(0, 0)
            load_x(0, 1)
            sp.wait_ge(zeroed, 3)
            move_k(0, 0)

            def body(n, first, last):
                for s in range(SLOTS):
                    b, j = divmod(s, PAIRS)
                    if j == 0:
                        if not (last and b + 3 >= BLOCKS):
                            load_y(n, b + 3)
                        load_mask_b(n, b)
                        if not (last and b + 2 >= BLOCKS):
                            load_mask_r(n, b + 2)
                    for start, load in ((S_SPLIT_T + 1, load_yt), (S_X + 1, load_x)):
                        q = s - start + 2
                        if 2 <= q < 6 and not (last and q >= 4):
                            load(n, q)
                    if j == 1 and not (last and b + 1 >= BLOCKS):
                        move_k(n, b + 1)
                    if not first and T_STORE <= s < T_STORE + 2:
                        for q in (2 * (s - T_STORE), 2 * (s - T_STORE) + 1):
                            store(n - 1, q)

            over_samples(sp, body)
            for q in range(BLOCKS):
                store(SAMPLES - 1, q)
            sp.wait_ge(stored, 16 * BLOCKS * SAMPLES)

        @block.tensor
        def _(pe):
            mm = nc.tensor.matmul

            def three_pass(dst, parts):
                todo = [(lh[a], rh[c]) for lh, rh in parts for a, c in ((0, 0), (0, 1), (1, 0))]
                for i, (lhs, rhs) in enumerate(todo):
                    last = mm(dst, lhs, rhs, start=i == 0, stop=i == len(todo) - 1)
                return last

            def scores(n, s):
                b, j = divmod(s, PAIRS)
                if j == 0:
                    pe.wait_ge(qkv_copied, count(n, 24, 6 * b + 1))
                    pe.wait_ge(k_moved[b % 2], count(n, 2, b // 2, 8 * 16))
                    pe.wait_ge(blocked_done, count(n, 4, b))
                if exists(n, 16, s - 2):
                    pe.wait_ge(shifted, count(n, 16, s - 2))
                dst = s_ps[s % 2]
                mm(dst[:, :].rearrange("p (h k) -> p h k", h=HEADS), neg_sel[:, :],
                   blocked[:, b % 2, j, :].unsqueeze(1).to_broadcast([P, HEADS, CHUNK]), start=True, stop=False)
                for hp in range(HP):
                    last = mm(dst[:, hp * P:(hp + 1) * P].rearrange("p (h k) -> p h k", h=2),
                              q_st[:, b % 2, hp, j, :, :].rearrange("p c q -> p (c q)"),
                              k_bd[:, b % 2, hp, :, j * CHUNK:(j + 1) * CHUNK], start=False, stop=hp == HP - 1)
                last.then_inc(scores_ready, 1)

            def transpose(n, s):
                pe.wait_ge(probs_done, count(n, 16, s))
                if exists(n, 16, s - 1):
                    pe.wait_ge(pt_copied, count(n, 16, s - 1))
                for hp in range(HP):
                    last = nc.tensor.transpose(pt_ps[:, hp, :], prob[:, s % RING, 2 * hp:2 * hp + 2, :].rearrange("p h k -> p (h k)"), ident)
                last.then_inc(transposed, 1)

            def values(n, s):
                b, j = divmod(s, PAIRS)
                pe.wait_ge(qkv_copied, count(n, 24, 6 * b + 5))
                pe.wait_ge(pt_copied, count(n, 16, s))
                if exists(n, 16, s - 1):
                    pe.wait_ge(att_lo_done, count(n, 16, s - 1))
                for hp in (0, 2, 1, 3):
                    for c in range(2):
                        w = v_bd[:, b % 2, j, c, hp, :, :].rearrange("p h d -> p (h d)")
                        last = mm(av_ps[64 * (hp % 2):64 * (hp % 2) + 64, hp // 2, c * CHUNK:(c + 1) * CHUNK], w,
                                  prob_t[:, s % 2, hp, c * CHUNK:(c + 1) * CHUNK], start=True, stop=True)
                last.then_inc(av_ready, 1)

            def wpair(which, i, o0, on):
                return w1_hi[:, which, i, o0:o0 + on], w1_lo[:, which, i, o0:o0 + on]

            def qk(n, b, which, g):
                bank = g
                if which == Q_W and g == 0:
                    pe.wait_ge(y_hi_done, count(n, 4, b))
                    pe.wait_ge(y_lo_done, count(n, 4, b))
                    if exists(n, 24, 6 * (b - 1) + 5):
                        pe.wait_ge(qkv_copied, count(n, 24, 6 * (b - 1) + 5))
                elif which == Q_W:
                    if exists(n, 8, 2 * (b - 3) + 1):
                        pe.wait_ge(u_done, count(n, 8, 2 * (b - 3) + 1))
                else:
                    pe.wait_ge(qkv_copied, count(n, 24, 6 * b + g))
                three_pass(pj_ps[bank][:, :], [(wpair(which, i, g * P, P), (y_hi[:, b % 2, i, :], y_lo[:, b % 2, i, :]))
                                               for i in range(HALVES)]).then_inc(qkv_ready, 1)

            def v(n, b, m):
                pe.wait_ge(qkv_copied, count(n, 24, 6 * b + (2 if m == 0 else 4)))
                for t in range(2):
                    cut = slice((2 * m + t) * P, (2 * m + t + 1) * P)
                    last = three_pass(pj_ps[0][:, t * E:(t + 1) * E],
                                      [((y_hi[:, b % 2, i, cut], y_lo[:, b % 2, i, cut]), wpair(V_W, i, 0, E)) for i in range(HALVES)])
                last.then_inc(qkv_ready, 1)

            def wout(n, b, o):
                pe.wait_ge(att_hi_done, count(n, 16, 4 * b + 3))
                pe.wait_ge(att_lo_done, count(n, 16, 4 * b + 3))
                if o == 1:
                    pe.wait_ge(u_done, count(n, 8, 2 * b))
                elif not (isinstance(n, int) and 4 * n + b + 2 >= BLOCKS * SAMPLES):
                    pe.wait_ge(qkv_copied, count(n, 24, 6 * (b + 2) + 3))
                else:
                    if exists(n, 8, 2 * (b - 1) + 1):
                        pe.wait_ge(u_done, count(n, 8, 2 * (b - 1) + 1))
                three_pass(pj_ps[1][:, :], [(wpair(O_W, i, o * P, P), (att_hi[:, b % 2, i, :], att_lo[:, b % 2, i, :]))
                                            for i in range(HALVES)]).then_inc(wout_ready, 1)

            def gram_part(n, q):
                pe.wait_ge(yt_hi_done, count(n, 4, q))
                pe.wait_ge(yt_lo_done, count(n, 4, q))
                if q == 0:
                    if exists(n - 1, 1, 0):
                        pe.wait_ge(gn_step, count(n - 1, 1, 0))
                for lb in range(PAIRS):
                    for i in range(HALVES):
                        last = mm(l0_ps[i][:, :].rearrange("p (a c) -> p a c", a=2), yt_hl[:, lb, 0, i * P:(i + 1) * P], yt_hl[:, lb, :, :],
                                  start=q == 0 and lb == 0, stop=q == BLOCKS - 1 and lb == PAIRS - 1)
                last.then_inc(gram_ready, 1)

            def layer0(n, s):
                if s == S_HLT:
                    pe.wait_ge(gram_half, count(n, 1, 0))
                    for i in range(HALVES):
                        for k in range(HALVES):
                            last = nc.tensor.transpose(l0_ps[0][:, i * E + k * P:i * E + (k + 1) * P], hl[:, k, i * P:(i + 1) * P], ident)
                    last.then_inc(hlt_ready, 1)
                elif s == S_T1:
                    pe.wait_ge(gram_done, count(n, 1, 0))
                    pe.wait_ge(y_sum_done, count(n, 1, 0))
                    for i in range(HALVES):
                        for k in range(HALVES):
                            mm(l0_ps[1][:, i * E:(i + 1) * E], gram[:, k, i * P:(i + 1) * P], w0_sb[:, K_W, k, :], start=k == 0, stop=k == 1)
                    for k in range(HALVES):
                        last = mm(l0_ps[0][:, 0:E], y_sum_b[:, k, :], w0_sb[:, K_W, k, :], start=k == 0, stop=k == 1)
                    last.then_inc(t1_ready, 1)
                elif s == S_SC:
                    pe.wait_ge(t1_done, count(n, 1, 0))
                    for i in range(HALVES):
                        for k in range(HALVES):
                            last = mm(l0_ps[0][:, i * P:(i + 1) * P], w0_sb[:, Q_W, k, i * P:(i + 1) * P], t1[:, k, i * P:(i + 1) * P],
                                      start=k == 0, stop=k == 1)
                    last.then_inc(sc0_ready, 1)
                elif s == S_U:
                    pe.wait_ge(a0_done, count(n, 1, 0))
                    for i in range(HALVES):
                        last = mm(l0_ps[1][:, i * E:(i + 1) * E], a0[:, i, :], w0_sb[:, O_W, i, :], start=True, stop=True)
                    last.then_inc(u0_ready, 1)
                elif s == S_M:
                    pe.wait_ge(u0_copied, count(n, 1, 0))
                    for k in range(HALVES):
                        for i in range(HALVES):
                            mm(l0_ps[0][:, k * E:(k + 1) * E], w0_sb[:, V_W, i, k * P:(k + 1) * P], u0[:, i, :], start=i == 0, stop=i == 1)
                    for k in range(HALVES):
                        for i in range(HALVES):
                            last = mm(l0_ps[1][:, k:k + 1], u0[:, i, k * P:(k + 1) * P], col[:, V_BV0, i:i + 1], start=i == 0, stop=i == 1)
                    last.then_inc(m_ready, 1)

            def layer0_output(n, q):
                pe.wait_ge(x_hi_done, count(n, 4, q))
                pe.wait_ge(x_lo_done, count(n, 4, q))
                if q == 0:
                    pe.wait_ge(m_lo_done, count(n, 1, 0))
                    pe.wait_ge(o_bias_done, count(n, 1, 0))
                for o in range(HALVES):
                    if exists(n, 8, 2 * q + o - 2):
                        pe.wait_ge(o_copied, count(n, 8, 2 * q + o - 2))
                    three_pass(l0_ps[o][:, :], [((m_hi[:, i, o * P:(o + 1) * P], m_lo[:, i, o * P:(o + 1) * P]), (x_hi[:, i, :], x_lo[:, i, :]))
                                                for i in range(HALVES)]).then_inc(mx_ready, 1)

            def mean_over_partitions(n):
                pe.wait_ge(o_aggr, count(n, 1, 0))
                mm(l0_ps[0][:, 0:1], mean_mat, o_mv[:, 0:1], start=True, stop=True).then_inc(mean_ready, 1)

            def variance_over_partitions(n):
                pe.wait_ge(dev_done, count(n, 1, 0))
                mm(l0_ps[0][:, 1:2], mean_mat, o_dev[:, 1:2], start=True, stop=True).then_inc(var_ready, 1)

            pe.wait_ge(weights_in, 5 * 16)
            w_raw = u_sb[:, :, :].rearrange("p h t -> p (h t)")[:, 0:4 * HALVES * E].rearrange("p (w h o) -> p w h o", w=4, h=HALVES)
            for o in range(HALVES):
                for i in range(HALVES):
                    last = mm(l0_ps[0][:, o:o + 1], w_raw[:, O_W, i, o * P:(o + 1) * P], col[:, V_BV1, i:i + 1], start=i == 0, stop=i == 1)
            last.then_inc(c1_ready, 1)
            pe.wait_ge(w_hi_done, 1)
            pe.wait_ge(w_lo_done, 1)
            pe.wait_ge(consts_done, 1)
            for g in range(2):
                qk(0, 0, Q_W, g)
            for g in range(2):
                qk(0, 0, K_W, g)
            for m in range(2):
                v(0, 0, m)
            pe.wait_ge(zeroed, 3)

            def body(n, first, last):
                for s in range(SLOTS):
                    b, j = divmod(s, PAIRS)
                    scores(n, s)
                    if not (first and s < LAG):
                        transpose(n, s - LAG)
                    if s == 0 and not first:
                        mean_over_partitions(n - 1)
                    if S_GRAM <= s < S_GRAM + BLOCKS:
                        gram_part(n, s - S_GRAM)
                    if S_MX <= s < S_MX + BLOCKS:
                        layer0_output(n, s - S_MX)
                    ahead = not (last and b + 1 >= BLOCKS)
                    if ahead and j < 2:
                        for g in range(2):
                            qk(n, b + 1, (Q_W, K_W)[j], g)
                    elif ahead:
                        v(n, b + 1, j - 2)
                    layer0(n, s)
                    if j >= 2 and not (first and b == 0):
                        wout(n, b - 1, j - 2)
                    if not (first and s < LAG):
                        values(n, s - LAG)
                    if s == 0 and not first:
                        variance_over_partitions(n - 1)

            over_samples(pe, body)
            n = SAMPLES - 1
            mean_over_partitions(n)
            for s in range(SLOTS - LAG, SLOTS):
                transpose(n, s)
                values(n, s)
            for o in range(HALVES):
                wout(n, BLOCKS - 1, o)
            variance_over_partitions(n)

        @block.scalar
        def _(act):
            copy = nc.scalar.copy

            def split_y(n, b):
                act.wait_ge(y_in[b % 2], count(n, 2, b // 2, 16))
                if exists(n, 24, 6 * (b - 2) + 5):
                    act.wait_ge(qkv_ready, count(n, 24, 6 * (b - 2) + 5))
                if b % 4 == 0:
                    if exists(n, 1, b // 4 - 1):
                        act.wait_ge(y_sum_done, count(n, 1, b // 4 - 1))
                for i in range(HALVES):
                    last = nc.scalar.activation(y_hi[:, b % 2, i, :], y_raw[:, b % 2, i, :], ACT.Copy,
                                                accum_out=y_sums[:, i, b % 4:b % 4 + 1])
                last.then_inc(y_hi_done, 1)

            def split_yt(n, q):
                act.wait_ge(yt_in[q % 2], count(n, 2, q // 2, 16))
                if exists(n, 4, q - 1):
                    act.wait_ge(gram_ready, count(n, 4, q - 1))
                copy(yt_hl[:, :, 0, :], yt_raw[:, q % 2]).then_inc(yt_hi_done, 1)

            def split_x(n, q):
                act.wait_ge(x_in[q % 2], count(n, 2, q // 2, 16))
                if exists(n, 8, 2 * (q - 1) + 1):
                    act.wait_ge(mx_ready, count(n, 8, 2 * (q - 1) + 1))
                copy(x_hi[:, :, :], x_raw[:, q % 2]).then_inc(x_hi_done, 1)

            def copy_q(n, b, g):
                act.wait_ge(qkv_ready, count(n, 24, 6 * b + g))
                if g == 0:
                    if exists(n, 16, 4 * (b - 2) + 3):
                        act.wait_ge(scores_ready, count(n, 16, 4 * (b - 2) + 3))
                for par in range(2):
                    rows = slice(64 * par, 64 * par + 64)
                    for c in range(2):
                        last = nc.scalar.activation(q_st[64 * c:64 * c + 64, b % 2, 2 * g + par, :, c, :],
                                                    pj_ps[g][rows, :].rearrange("p (r c k) -> p r c k", c=2, k=CHUNK)[:, :, c, :],
                                                    ACT.Identity, bias=col[rows, V_BQ1, g:g + 1])
                last.then_inc(qkv_copied, 1)

            def copy_k(n, b, g):
                act.wait_ge(qkv_ready, count(n, 24, 6 * b + 2 + g))
                if g == 0:
                    if exists(n, 2, (b - 1) // 2):
                        act.wait_ge(k_moved[(b - 1) % 2], count(n, 2, (b - 1) // 2, 16 * 8))
                nc.scalar.activation(k_s[:, g, :, :].rearrange("p c (r k) -> p r c k", k=CHUNK),
                                     pj_ps[g][:, :].rearrange("p (r c k) -> p r c k", c=2, k=CHUNK), ACT.Identity,
                                     bias=col[:, V_BK1, g:g + 1]).then_inc(qkv_copied, 1)

            def copy_v(n, b, m):
                act.wait_ge(qkv_ready, count(n, 24, 6 * b + 4 + m))
                if m == 0:
                    if exists(n, 16, 4 * (b - 2) + 3):
                        act.wait_ge(av_ready, count(n, 16, 4 * (b - 2) + 3))
                for c in range(2):
                    src = pj_ps[0][64 * c:64 * c + 64, :].rearrange("p (t q h d) -> p t q h d", t=2, q=HP, h=2)
                    for h in range(2):
                        last = copy(v_bd[64 * h:64 * h + 64, b % 2, 2 * m:2 * m + 2, c, :, h, :], src[:, :, :, h, :])
                last.then_inc(qkv_copied, 1)

            def copy_pt(n, s):
                act.wait_ge(transposed, count(n, 16, s))
                if exists(n, 16, s - 2):
                    act.wait_ge(av_ready, count(n, 16, s - 2))
                copy(prob_t[:, s % 2], pt_ps[:, :, :]).then_inc(pt_copied, 1)

            def exponents(n, s):
                act.wait_ge(shifted, count(n, 16, s))
                nc.scalar.activation(prob[:, s % RING], prob[:, s % RING], ACT.Exp, scale=SCALE1).then_inc(exp_done, 1)

            def group_normed(n, q):
                if q == 0:
                    act.wait_ge(gn_done, count(n, 1, 0))
                act.wait_ge(o_stats_done, count(n, 8, 2 * q + 1))
                for o in range(HALVES):
                    cut = o_sb[:, o, q * BT:(q + 1) * BT]
                    last = nc.scalar.activation(cut, cut, ACT.Identity, scale=gn[:, 0, o:o + 1], bias=gn[:, 1, o:o + 1])
                last.then_inc(x1_done, 1)

            def copy_att(n, s):
                b, j = divmod(s, PAIRS)
                act.wait_ge(av_ready, count(n, 16, s))
                if j == 0:
                    if exists(n, 8, 2 * (b - 2) + 1):
                        act.wait_ge(wout_ready, count(n, 8, 2 * (b - 2) + 1))
                copy(att_hi[:, b % 2, :, j * P:(j + 1) * P], av_ps[:, :, :]).then_inc(att_hi_done, 1)

            def layer0_exponents(n):
                act.wait_ge(a0_shift, count(n, 1, 0))
                for i in range(HALVES):
                    last = nc.scalar.activation(a0[:, i, :], a0[:, i, :], ACT.Exp, bias=a0_max[:, i:i + 1], scale=SCALE0,
                                                accum_out=a0_sum[:, i:i + 1])
                last.then_inc(a0_exp, 1)

            def copy_output(n, q):
                if q == 0:
                    if exists(n - 1, 4, 3):
                        act.wait_ge(stored, count(n - 1, 4, 3, 16))
                for o in range(HALVES):
                    act.wait_ge(mx_ready, count(n, 8, 2 * q + o))
                    nc.scalar.activation(o_sb[:, o, q * BT:(q + 1) * BT], l0_ps[o][:, :], ACT.Identity,
                                         bias=o_bias[:, o:o + 1]).then_inc(o_copied, 1)

            def copy_hl(n):
                act.wait_ge(gram_ready, count(n, 4, 3))
                for i in range(HALVES):
                    last = copy(hl[:, i, :], l0_ps[i][:, E:2 * E])
                last.then_inc(hl_copied, 1)

            def copy_u0(n):
                act.wait_ge(u0_ready, count(n, 1, 0))
                copy(u0[:, :, :], l0_ps[1][:, :].rearrange("p (i o) -> p i o", i=HALVES)).then_inc(u0_copied, 1)

            act.wait_ge(weights_in, 5 * 16)
            w_raw = u_sb[:, :, :].rearrange("p h t -> p (h t)")[:, 0:4 * HALVES * E]
            copy(w1_hi[:, :, :, :].rearrange("p w h o -> p (w h o)"), w_raw).then_inc(w_hi_done, 1)
            nc.scalar.mul(bk_l[:, :], bk_row[:, :], float(L)).then_inc(consts_done, 1)
            split_y(0, 0)
            split_y(0, 1)
            act.wait_ge(zeroed, 3)
            for g in range(2):
                copy_q(0, 0, g)
            for g in range(2):
                copy_k(0, 0, g)
            for m in range(2):
                copy_v(0, 0, m)

            def body(n, first, last):
                for s in range(SLOTS):
                    b, j = divmod(s, PAIRS)
                    if not (first and s < LAG):
                        copy_pt(n, s - LAG)
                    if s == S_HL:
                        copy_hl(n)
                    if s == S_SC + 1:
                        layer0_exponents(n)
                    if S_MX <= s < S_MX + BLOCKS:
                        copy_output(n, s - S_MX)
                    if S_X <= s < S_X + BLOCKS:
                        split_x(n, s - S_X)
                    if S_SPLIT_T <= s < S_SPLIT_T + BLOCKS:
                        split_yt(n, s - S_SPLIT_T)
                    ahead = not (last and b + 1 >= BLOCKS)
                    if ahead and j < 2:
                        for g in range(2):
                            (copy_q, copy_k)[j](n, b + 1, g)
                    elif ahead:
                        copy_v(n, b + 1, j - 2)
                    exponents(n, s)
                    if not (first and s < LAG):
                        copy_att(n, s - LAG)
                    if j == 1 and not (last and b + 2 >= BLOCKS):
                        split_y(n, b + 2)
                    if s == S_U:
                        copy_u0(n)
                    if not first and T_X1 <= s < T_X1 + BLOCKS:
                        group_normed(n - 1, s - T_X1)

            over_samples(act, body)
            for s in range(SLOTS - LAG, SLOTS):
                copy_pt(SAMPLES - 1, s)
                copy_att(SAMPLES - 1, s)
            for q in range(BLOCKS):
                group_normed(SAMPLES - 1, q)

        @block.vector
        def _(dve):
            tt, stt = nc.vector.tensor_tensor, nc.vector.scalar_tensor_tensor

            def split_y(n, b):
                dve.wait_ge(y_hi_done, count(n, 4, b))
                tt(y_lo[:, b % 2], y_raw[:, b % 2], y_hi[:, b % 2], ALU.subtract).then_inc(y_lo_done, 1)

            def split_yt(n, q):
                dve.wait_ge(yt_hi_done, count(n, 4, q))
                tt(yt_hl[:, :, 1, :], yt_raw[:, q % 2], yt_hl[:, :, 0, :], ALU.subtract).then_inc(yt_lo_done, 1)

            def split_x(n, q):
                dve.wait_ge(x_hi_done, count(n, 4, q))
                tt(x_lo[:, :, :], x_raw[:, q % 2], x_hi[:, :, :], ALU.subtract).then_inc(x_lo_done, 1)

            def flags(n, b):
                dve.wait_ge(mask_r_in[b % 2], count(n, 2, b // 2, 3 * 16))
                if exists(n, 16, 4 * (b - 2) + 3):
                    dve.wait_ge(scores_ready, count(n, 16, 4 * (b - 2) + 3))
                nc.vector.tensor_scalar(blocked[0:6, b % 2], mask_r[:, b % 2], 0.0, None, ALU.is_le).then_inc(blocked_done, 1)

            def shift(n, s):
                dve.wait_ge(scores_ready, count(n, 16, s))
                src = s_ps[s % 2][:, :].rearrange("p (h k) -> p h k", h=HEADS)
                nc.vector.tensor_reduce(row_max[:, s % RING, :], src, AX.X, ALU.max).then_inc(max_done, 1)
                dve.wait_ge(max_done, count(n, 16, s))
                if exists(n, 16, s - RING):
                    dve.wait_ge(transposed, count(n, 16, s - RING))
                tt(prob[:, s % RING], src, row_max[:, s % RING, :].unsqueeze(2).to_broadcast([P, HEADS, CHUNK]),
                   ALU.subtract).then_inc(shifted, 1)

            def sums(n, s):
                dve.wait_ge(exp_done, count(n, 16, s))
                nc.vector.tensor_reduce(row_sum[:, s % RING, :], prob[:, s % RING], AX.X, ALU.add).then_inc(sum_done, 1)
                dve.wait_ge(sum_done, count(n, 16, s))
                if exists(n, 16, s - RING):
                    dve.wait_ge(probs_done, count(n, 16, s - RING))
                nc.vector.reciprocal(row_inv[:, s % RING, :], row_sum[:, s % RING, :]).then_inc(inv_done, 1)

            def att_low(n, s):
                b, j = divmod(s, PAIRS)
                dve.wait_ge(att_hi_done, count(n, 16, s))
                cut = slice(j * P, (j + 1) * P)
                tt(att_lo[:, b % 2, :, cut], av_ps[:, :, :], att_hi[:, b % 2, :, cut], ALU.subtract).then_inc(att_lo_done, 1)

            def branch(n, b, o):
                dve.wait_ge(wout_ready, count(n, 8, 2 * b + o))
                if o == 0:
                    dve.wait_ge(mask_b_in[b % 2], count(n, 2, b // 2, 16))
                stt(out=u_sb[:, o, (b % 4) * BT:(b % 4 + 1) * BT], in0=pj_ps[1][:, :], scalar=c1[:, o:o + 1], in1=mask_b[:, b % 2, :],
                    op0=ALU.add, op1=ALU.mult).then_inc(u_done, 1)

            def layer0(n, s):
                if s == S_HL:
                    dve.wait_ge(hl_copied, count(n, 1, 0))
                    for i in range(HALVES):
                        last = tt(gram[:, i, :], l0_ps[i][:, 0:E], hl[:, i, :], ALU.add)
                    last.then_inc(gram_half, 1)
                elif s == S_HLT:
                    dve.wait_ge(hlt_ready, count(n, 1, 0))
                    tt(gram[:, :, :], l0_ps[0][:, :].rearrange("p (i c) -> p i c", i=HALVES), gram[:, :, :], ALU.add).then_inc(gram_done, 1)
                elif s == S_SUM:
                    dve.wait_ge(y_hi_done, count(n, 4, 3))
                    nc.vector.tensor_reduce(y_sum[:, :], y_sums[:, :, :], AX.X, ALU.add).then_inc(y_sum_step, 1)
                    dve.wait_ge(y_sum_step, count(n, 1, 0))
                    nc.vector.tensor_copy(y_sum_b[:, :, :], y_sum[:, :].unsqueeze(2).to_broadcast([P, HALVES, P])).then_inc(y_sum_done, 1)
                elif s == S_T1:
                    dve.wait_ge(t1_ready, count(n, 1, 0))
                    for i in range(HALVES):
                        stt(out=t1[:, i, :], in0=bk_row[:, :], scalar=y_sum[:, i:i + 1], in1=l0_ps[1][:, i * E:(i + 1) * E],
                            op0=ALU.mult, op1=ALU.add)
                    tt(v_row[:, :], l0_ps[0][:, 0:E], bk_l[:, :], ALU.add).then_inc(t1_done, 1)
                elif s == S_SC:
                    dve.wait_ge(sc0_ready, count(n, 1, 0))
                    dve.wait_ge(t1_done, count(n, 1, 0))
                    for i in range(HALVES):
                        last = stt(out=a0[:, i, :], in0=v_row[:, i * P:(i + 1) * P], scalar=col[:, V_BQ0, i:i + 1],
                                   in1=l0_ps[0][:, i * P:(i + 1) * P], op0=ALU.mult, op1=ALU.add)
                    last.then_inc(a0_step, 1)
                    dve.wait_ge(a0_step, count(n, 4, 0))
                    tt(a0[:, :, :], a0[:, :, :], head_mask.unsqueeze(1).to_broadcast([P, HALVES, P]), ALU.add).then_inc(a0_step, 1)
                    dve.wait_ge(a0_step, count(n, 4, 1))
                    nc.vector.tensor_reduce(a0_max[:, :], a0[:, :, :], AX.X, ALU.max).then_inc(a0_step, 1)
                    dve.wait_ge(a0_step, count(n, 4, 2))
                    nc.vector.tensor_scalar(a0_max[:, :], a0_max[:, :], -SCALE0, None, ALU.mult).then_inc(a0_shift, 1)
                elif s == S_M:
                    dve.wait_ge(m_ready, count(n, 1, 0))
                    tt(m_t[:, :, :], l0_ps[0][:, :].rearrange("p (i o) -> p i o", i=HALVES), resid, ALU.add).then_inc(m_done, 1)
                    dve.wait_ge(m_done, count(n, 1, 0))
                    nc.vector.tensor_copy(m_hi[:, :, :], m_t[:, :, :]).then_inc(m_hi_done, 1)
                    dve.wait_ge(m_hi_done, count(n, 1, 0))
                    tt(m_lo[:, :, :], m_t[:, :, :], m_hi[:, :, :], ALU.subtract).then_inc(m_lo_done, 1)
                    tt(o_bias[:, :], l0_ps[1][:, 0:HALVES], col[:, V_BO0, :], ALU.add).then_inc(o_bias_done, 1)
                elif S_MX <= s < S_MX + BLOCKS:
                    q = s - S_MX
                    for o in range(HALVES):
                        dve.wait_ge(o_copied, count(n, 8, 2 * q + o))
                        nc.vector.bn_stats(o_stats[:, HALVES * q + o, :], o_sb[:, o, q * BT:(q + 1) * BT]).then_inc(o_stats_done, 1)

            def layer0_normalize(n):
                dve.wait_ge(a0_exp, count(n, 1, 0))
                nc.vector.reciprocal(a0_sum[:, :], a0_sum[:, :]).then_inc(a0_step, 1)
                dve.wait_ge(a0_step, count(n, 4, 3))
                tt(a0[:, :, :], a0[:, :, :], a0_sum[:, :].unsqueeze(2).to_broadcast([P, HALVES, P]), ALU.mult).then_inc(a0_done, 1)

            def group_mean(n):
                dve.wait_ge(o_stats_done, count(n, 8, 7))
                nc.vector.tensor_copy(carrier[:, 0:1], ident[:, 0:1])
                nc.vector.bn_aggr(o_mv[:, :], o_stats[:, :, :].rearrange("p a b -> p (a b)")).then_inc(o_aggr, 1)

            def group_deviation(n):
                dve.wait_ge(mean_ready, count(n, 1, 0))
                dve.wait_ge(o_aggr, count(n, 1, 0))
                nc.vector.tensor_copy(o_mu[:, :], l0_ps[0][:, 0:1])
                tt(o_dev[:, 0:1], o_mv[:, 0:1], l0_ps[0][:, 0:1], ALU.subtract).then_inc(dev_step, 1)
                dve.wait_ge(dev_step, count(n, 1, 0))
                stt(out=o_dev[:, 1:2], in0=o_dev[:, 0:1], scalar=o_dev[:, 0:1], in1=o_mv[:, 1:2], op0=ALU.mult, op1=ALU.add).then_inc(dev_done, 1)

            def group_variance(n):
                dve.wait_ge(var_ready, count(n, 1, 0))
                nc.vector.tensor_scalar(o_var[:, :], l0_ps[0][:, 1:2], EPS, None, ALU.add).then_inc(gn_step, 1)

            def stats_of_z(n, q):
                dve.wait_ge(z_done, count(n, 4, q))
                for o in range(HALVES):
                    nc.vector.bn_stats(z_stats[:, o, q, :], o_sb[:, o, q * BT:(q + 1) * BT]).then_inc(z_stats_done, 1)

            def instance_norm(n):
                dve.wait_ge(z_stats_done, count(n, 8, 7))
                nc.vector.tensor_copy(carrier[:, 0:1], ident[:, 0:1])
                for o in range(HALVES):
                    last = nc.vector.bn_aggr(z_mv[:, o, :], z_stats[:, o, :, :].rearrange("p a b -> p (a b)"))
                last.then_inc(z_step, 1)
                dve.wait_ge(z_step, count(n, 1, 0))
                nc.vector.tensor_scalar(z_var[:, :], z_mv[:, :, 1], EPS, None, ALU.add).then_inc(z_norm_step, 1)

            def result(n, q):
                if q == 0:
                    dve.wait_ge(z_norm_done, count(n, 1, 0))
                for o in range(HALVES):
                    cut = o_sb[:, o, q * BT:(q + 1) * BT]
                    last = nc.vector.tensor_scalar(cut, cut, z_rstd[:, o:o + 1], z_shift[:, o:o + 1], ALU.mult, ALU.subtract)
                last.then_inc(final_done, 1)

            nc.vector.memset(blocked[:, :, :, :], 0.0).then_inc(blocked_zero, 1)
            nc.vector.memset(q_st[:, :, :, :, :, :], 0.0).then_inc(zeroed, 1)
            dve.wait_ge(blocked_zero, 1)
            flags(0, 0)
            dve.wait_ge(weights_in, 5 * 16)
            nc.vector.tensor_copy(neg_sel[:, :], cst[:, C_NEG:C_NEG + P])
            dve.wait_ge(c1_ready, 1)
            tt(c1[:, :], l0_ps[0][:, 0:HALVES], col[:, V_BO1, :], ALU.add).then_inc(c1_done, 1)
            dve.wait_ge(w_hi_done, 1)
            w_raw = u_sb[:, :, :].rearrange("p h t -> p (h t)")[:, 0:4 * HALVES * E]
            tt(w1_lo[:, :, :, :].rearrange("p w h o -> p (w h o)"), w_raw, w1_hi[:, :, :, :].rearrange("p w h o -> p (w h o)"),
               ALU.subtract).then_inc(w_lo_done, 1)
            split_y(0, 0)
            split_y(0, 1)
            dve.wait_ge(c1_done, 1)
            dve.wait_ge(consts_done, 1)

            def body(n, first, last):
                for s in range(SLOTS):
                    b, j = divmod(s, PAIRS)
                    if not (first and s < LAG + 1):
                        att_low(n, s - LAG - 1)
                    if j == 3 and not (first and b == 0):
                        branch(n, b - 1, 0)
                    if j == 0 and not (first and b < 2):
                        branch(n, b - 2, 1)
                    if not (first and s == 0):
                        sums(n, s - 1)
                    shift(n, s)
                    if s == 0 and not first:
                        group_deviation(n - 1)
                    if S_X <= s < S_X + BLOCKS:
                        split_x(n, s - S_X)
                    if S_SPLIT_T <= s < S_SPLIT_T + BLOCKS:
                        split_yt(n, s - S_SPLIT_T)
                    if j == 0 and not (last and b + 1 >= BLOCKS):
                        flags(n, b + 1)
                    if s == 0 and not first:
                        group_variance(n - 1)
                    if not first and T_Z_STATS <= s < T_Z_STATS + BLOCKS:
                        stats_of_z(n - 1, s - T_Z_STATS)
                    if not first and s == T_STAT:
                        instance_norm(n - 1)
                    if not first and T_FINAL <= s < T_FINAL + 2:
                        for q in (2 * (s - T_FINAL), 2 * (s - T_FINAL) + 1):
                            result(n - 1, q)
                    if s == S_SC + 1:
                        layer0_normalize(n)
                    if j == 1 and not (last and b + 2 >= BLOCKS):
                        split_y(n, b + 2)
                    layer0(n, s)
                group_mean(n)

            over_samples(dve, body)
            n = SAMPLES - 1
            att_low(n, SLOTS - LAG - 1)
            branch(n, BLOCKS - 2, 1)
            sums(n, SLOTS - 1)
            group_deviation(n)
            for s in range(SLOTS - LAG, SLOTS):
                att_low(n, s)
            for o in range(HALVES):
                branch(n, BLOCKS - 1, o)
            group_variance(n)
            for q in range(BLOCKS):
                stats_of_z(n, q)
            instance_norm(n)
            for q in range(BLOCKS):
                result(n, q)

        @block.gpsimd
        def _(pool):
            def scale_probs(n, s):
                pool.wait_ge(inv_done, count(n, 16, s))
                nc.gpsimd.tensor_tensor(prob[:, s % RING], prob[:, s % RING], row_inv[:, s % RING, :].unsqueeze(2).to_broadcast([P, HEADS, CHUNK]),
                                        ALU.mult).then_inc(probs_done, 1)

            def group_norm(n):
                pool.wait_ge(gn_step, count(n, 1, 0))
                nc.gpsimd.tensor_tensor(o_rstd[:, :], o_var[:, :], power[:, 0:1], ALU.pow).then_inc(gn_step2, 1)
                pool.wait_ge(gn_step2, count(n, 3, 0))
                nc.gpsimd.tensor_tensor(gn[:, 0, :], col[:, V_GW, :], o_rstd[:, 0:1].to_broadcast([P, HALVES]), ALU.mult).then_inc(gn_step2, 1)
                pool.wait_ge(gn_step2, count(n, 3, 1))
                nc.gpsimd.tensor_tensor(gn[:, 1, :], gn[:, 0, :], o_mu[:, 0:1].to_broadcast([P, HALVES]), ALU.mult).then_inc(gn_step2, 1)
                pool.wait_ge(gn_step2, count(n, 3, 2))
                nc.gpsimd.tensor_tensor(gn[:, 1, :], col[:, V_GB, :], gn[:, 1, :], ALU.subtract).then_inc(gn_done, 1)

            def join(n, q):
                pool.wait_ge(x1_done, count(n, 4, q))
                pool.wait_ge(u_done, count(n, 8, 2 * q + 1))
                cut = slice(q * BT, (q + 1) * BT)
                nc.gpsimd.tensor_tensor(o_sb[:, :, cut], o_sb[:, :, cut], u_sb[:, :, cut], ALU.add).then_inc(z_done, 1)

            def instance_norm(n):
                pool.wait_ge(z_norm_step, count(n, 1, 0))
                nc.gpsimd.tensor_tensor(z_rstd[:, :], z_var[:, :], power[:, :], ALU.pow).then_inc(z_rstd_done, 1)
                pool.wait_ge(z_rstd_done, count(n, 1, 0))
                nc.gpsimd.tensor_tensor(z_shift[:, :], z_mv[:, :, 0], z_rstd[:, :], ALU.mult).then_inc(z_norm_done, 1)

            nc.gpsimd.memset(power[:, :], -0.5).then_inc(power_set, 1)
            nc.gpsimd.memset(v_bd[:, :, :, :, :, :, :], 0.0).then_inc(zeroed, 1)
            nc.gpsimd.memset(k_bd[:, :, :, :, :], 0.0).then_inc(zeroed, 1)

            def body(n, first, last):
                for s in range(SLOTS):
                    if not (first and s == 0):
                        scale_probs(n, s - 1)
                    if s == 0 and not first:
                        group_norm(n - 1)
                    if not first and T_Z <= s < T_Z + BLOCKS:
                        join(n - 1, s - T_Z)
                    if s == T_STAT and not first:
                        instance_norm(n - 1)

            pool.wait_ge(power_set, 1)
            over_samples(pool, body)
            scale_probs(SAMPLES - 1, SLOTS - 1)
            group_norm(SAMPLES - 1)
            for q in range(BLOCKS):
                join(SAMPLES - 1, q)
            instance_norm(SAMPLES - 1)


def kernel(x, ctx_4096, mask_Bx1x4096_ff1, L0_xattn_Wq, L0_xattn_bq, L0_xattn_Wk, L0_xattn_bk, L0_xattn_Wv, L0_xattn_bv,
           L0_xattn_Wo, L0_xattn_bo, L0_xattn_gn_w, L0_xattn_gn_b, L1_xattn_W_in, L1_xattn_b_in, L1_xattn_W_out, L1_xattn_b_out):
    import numpy as np
    import concourse.bacc as bacc
    from concourse import mybir
    from concourse.bass_utils import run_bass_kernel_spmd

    def halves(w):
        return np.asarray(w).reshape(HALVES, P, -1).transpose(1, 0, 2)

    w_in = np.asarray(L1_xattn_W_in)
    b_in = np.asarray(L1_xattn_b_in)
    w0 = np.stack([halves(np.asarray(L0_xattn_Wq).T), halves(np.asarray(L0_xattn_Wk).T), halves(L0_xattn_Wv),
                   halves(np.asarray(L0_xattn_Wo).T)], axis=1)
    w1 = np.zeros((P, HALVES * L), np.float32)
    w1[:, :4 * HALVES * E] = np.stack([halves(w_in[:E].T), halves(w_in[E:2 * E].T), halves(w_in[2 * E:].T),
                                       halves(np.asarray(L1_xattn_W_out).T)], axis=1).reshape(P, -1)
    cols = np.stack([halves(v)[:, :, 0] for v in (L0_xattn_bq, L0_xattn_bv, L0_xattn_bo, L0_xattn_gn_w, L0_xattn_gn_b,
                                                  b_in[:E], b_in[E:2 * E], b_in[2 * E:], L1_xattn_b_out)], axis=1)
    consts = np.zeros((P, C_ALL), np.float32)
    consts[:, C_IDENT:C_IDENT + P] = np.eye(P)
    consts[:, C_HEAD:C_HEAD + P] = np.where(np.arange(P)[:, None] // DH == np.arange(P)[None, :] // DH, 0.0, OFF_HEAD)
    for j in range(HALVES):
        consts[:, C_RESID + j * E + j * P:C_RESID + j * E + (j + 1) * P] = np.eye(P)
    consts[:, C_MEAN:C_MEAN + P] = 1.0 / P
    rest = np.float32(NEG / SCALE1)
    for part in range(3):
        piece = (np.array([rest], np.float32).view(np.uint32) & np.uint32(0xFFFF0000)).view(np.float32)[0]
        rest = np.float32(rest - piece)
        for c in range(2):
            consts[2 * part + c, C_NEG + c * CHUNK:C_NEG + (c + 1) * CHUNK] = piece

    given = {
        "x": np.asarray(x), "ctx": np.asarray(ctx_4096), "ctx_t": np.asarray(ctx_4096).transpose(0, 2, 1),
        "mask": np.asarray(mask_Bx1x4096_ff1), "w0": w0, "w1": w1, "cols": cols,
        "bk0": np.asarray(L0_xattn_bk).reshape(1, E), "consts": consts,
    }
    nc = bacc.Bacc("TRN2", target_bir_lowering=False, num_devices=1, dynamic_dma_scratch_size=1024)
    arrays, args = {}, {}
    for name, a in given.items():
        arrays[f"in_{name}"] = np.ascontiguousarray(a)
        args[name] = nc.dram_tensor(f"in_{name}", a.shape, mybir.dt.float32, kind="ExternalInput").ap()
    args["out"] = nc.dram_tensor("out_z", (SAMPLES, E, L), mybir.dt.float32, kind="ExternalOutput").ap()
    build(nc, **args)
    return run_bass_kernel_spmd(nc, [arrays], core_ids=[0]).results[0]["out_z"]
```
